# Optimizing a Trainium2 kernel written in Bass

```python
import numpy as np
import jax
import jax.numpy as jnp

def _softmax(x, axis=-1):
    return jax.nn.softmax(x, axis=axis)

def _gelu(x):
    return jax.nn.gelu(x, approximate=True)

def _silu(x):
    return jax.nn.silu(x)

def _sigmoid(x):
    return jax.nn.sigmoid(x)

def _layernorm(x, axis=-1, eps=1e-05):
    m = jnp.mean(x, axis=axis, keepdims=True)
    v = jnp.var(x, axis=axis, keepdims=True)
    return (x - m) / jnp.sqrt(v + eps)

def _scatter_add(tgt, idx, src, axis=0):
    return tgt.at[idx].add(src)

def _segment_sum(src, seg, n):
    return jax.ops.segment_sum(src, seg, n)
kernel_name = 'mk_seq_postln_d1_jaxref_r8_a02440'

def setup_inputs(seed: int=0):
    np.random.seed(seed)
    _w = jnp.asarray

    def _L0_attn_setup():
        import jax, jax.numpy as jnp
        import numpy as np
        import math
        D_MODEL = 128
        NUM_HEADS = 16
        D_HEAD = D_MODEL // NUM_HEADS
        N_FREQ = D_HEAD // 2 + 1
        COMPRESSION_RATIO = 0.5

        def _spectral_filter(t, mask):
            tf = jnp.fft.rfft(t, axis=-1)
            tf = tf * mask
            return jnp.fft.irfft(tf, n=t.shape[-1], axis=-1).astype(t.dtype)
        key = jax.random.key(seed)
        k_x, k_qkv, k_out, k_b, k_m = jax.random.split(key, 5)
        B, S = (2, 256)
        x = jax.random.normal(k_x, (B, S, D_MODEL), dtype=jnp.float32)
        w_qkv = jax.random.normal(k_qkv, (D_MODEL, 3 * D_MODEL), dtype=jnp.float32) / math.sqrt(D_MODEL)
        w_out = jax.random.normal(k_out, (D_MODEL, D_MODEL), dtype=jnp.float32) / math.sqrt(D_MODEL)
        b_out = jax.random.normal(k_b, (D_MODEL,), dtype=jnp.float32) * 0.01
        init_logit = math.log(COMPRESSION_RATIO / (1.0 - COMPRESSION_RATIO))
        mask_logits = init_logit + 0.1 * jax.random.normal(k_m, (N_FREQ,), dtype=jnp.float32)
        return {'x': x, 'w_qkv': w_qkv, 'w_out': w_out, 'b_out': b_out, 'mask_logits': mask_logits}
    _L0_attn_in = _L0_attn_setup()

    def _L0_ffn_setup():
        import jax, jax.numpy as jnp
        import numpy as np
        B, S, D, F, E = (2, 256, 128, 512, 8)
        LN_EPS = 1e-05

        def _layer_norm(x, gamma, beta):
            mu = jnp.mean(x, axis=-1, keepdims=True)
            var = jnp.mean(jnp.square(x - mu), axis=-1, keepdims=True)
            return (x - mu) * jax.lax.rsqrt(var + LN_EPS) * gamma + beta
        key = jax.random.key(seed)
        ks = jax.random.split(key, 8)

        def xavier(k, shape):
            fan_in, fan_out = (shape[-1], shape[-2])
            a = jnp.sqrt(6.0 / (fan_in + fan_out))
            return jax.random.uniform(k, shape, jnp.float32, -a, a)
        return {'tgt': jax.random.normal(ks[0], (B, S, D), jnp.float32), 'Wr': xavier(ks[1], (E, D)), 'br': jnp.zeros((E,), jnp.float32), 'W1': xavier(ks[2], (E, F, D)), 'b1': jnp.zeros((E, F), jnp.float32), 'W2': xavier(ks[3], (E, D, F)), 'b2': jnp.zeros((E, D), jnp.float32), 'gamma': jnp.ones((D,), jnp.float32), 'beta': jnp.zeros((D,), jnp.float32)}
    _L0_ffn_in = _L0_ffn_setup()
    _d = {'L0_attn_x': _L0_attn_in['x'], 'L0_attn_w_qkv': _L0_attn_in['w_qkv'], 'L0_attn_w_out': _L0_attn_in['w_out'], 'L0_attn_b_out': _L0_attn_in['b_out'], 'L0_attn_mask_logits': _L0_attn_in['mask_logits'], 'L0_ffn_Wr': _L0_ffn_in['Wr'], 'L0_ffn_br': _L0_ffn_in['br'], 'L0_ffn_W1': _L0_ffn_in['W1'], 'L0_ffn_b1': _L0_ffn_in['b1'], 'L0_ffn_W2': _L0_ffn_in['W2'], 'L0_ffn_b2': _L0_ffn_in['b2'], 'L0_ffn_gamma': _L0_ffn_in['gamma'], 'L0_ffn_beta': _L0_ffn_in['beta']}
    _x0 = _d['L0_attn_x']
    _d['L0_attn_x'] = jax.random.normal(jax.random.fold_in(jax.random.key(seed), 1), (8, 512, 128), dtype=_x0.dtype)
    del _x0
    return _d

def reference(L0_attn_x, L0_attn_w_qkv, L0_attn_w_out, L0_attn_b_out, L0_attn_mask_logits, L0_ffn_Wr, L0_ffn_br, L0_ffn_W1, L0_ffn_b1, L0_ffn_W2, L0_ffn_b2, L0_ffn_gamma, L0_ffn_beta):

    def _L0_attn_ref(x, w_qkv, w_out, b_out, mask_logits):
        import jax, jax.numpy as jnp
        import numpy as np
        import math
        D_MODEL = 128
        NUM_HEADS = 16
        D_HEAD = D_MODEL // NUM_HEADS
        N_FREQ = D_HEAD // 2 + 1
        COMPRESSION_RATIO = 0.5

        def _spectral_filter(t, mask):
            tf = jnp.fft.rfft(t, axis=-1)
            tf = tf * mask
            return jnp.fft.irfft(tf, n=t.shape[-1], axis=-1).astype(t.dtype)
        B, S, D = x.shape
        H, dh = (NUM_HEADS, D_HEAD)
        qkv = x @ w_qkv
        q, k, v = jnp.split(qkv, 3, axis=-1)
        to_heads = lambda t: t.reshape(B, S, H, dh).transpose(0, 2, 1, 3)
        q, k, v = (to_heads(q), to_heads(k), to_heads(v))
        mask = jax.nn.sigmoid(mask_logits)
        q = _spectral_filter(q, mask)
        k = _spectral_filter(k, mask)
        scores = jnp.einsum('bhqd,bhkd->bhqk', q, k) / math.sqrt(dh)
        attn = jax.nn.softmax(scores, axis=-1)
        out = jnp.einsum('bhqk,bhkd->bhqd', attn, v)
        out = out.transpose(0, 2, 1, 3).reshape(B, S, D)
        return out @ w_out + b_out

    def _L0_ffn_ref(tgt, Wr, br, W1, b1, W2, b2, gamma, beta):
        import jax, jax.numpy as jnp
        import numpy as np
        B, S, D, F, E = (2, 256, 128, 512, 8)
        LN_EPS = 1e-05

        def _layer_norm(x, gamma, beta):
            mu = jnp.mean(x, axis=-1, keepdims=True)
            var = jnp.mean(jnp.square(x - mu), axis=-1, keepdims=True)
            return (x - mu) * jax.lax.rsqrt(var + LN_EPS) * gamma + beta
        logits = jnp.einsum('bsd,ed->bse', tgt, Wr) + br
        top_v, top_i = jax.lax.top_k(logits, 2)
        top_w = jax.nn.softmax(top_v, axis=-1)
        n_exp = logits.shape[-1]
        router_w = jnp.sum(jax.nn.one_hot(top_i, n_exp, dtype=top_w.dtype) * top_w[..., None], axis=-2)
        h = jnp.einsum('bsd,efd->bsef', tgt, W1) + b1
        h = jax.nn.relu(h)
        o = jnp.einsum('bsef,edf->bsed', h, W2) + b2
        tgt2 = jnp.einsum('bsed,bse->bsd', o, router_w)
        return _layer_norm(tgt + tgt2, gamma, beta)
    x = L0_attn_x
    x = _layernorm(x + _L0_attn_ref(x, L0_attn_w_qkv, L0_attn_w_out, L0_attn_b_out, L0_attn_mask_logits), axis=-1)
    x = _layernorm(x + _L0_ffn_ref(x, L0_ffn_Wr, L0_ffn_br, L0_ffn_W1, L0_ffn_b1, L0_ffn_W2, L0_ffn_b2, L0_ffn_gamma, L0_ffn_beta), axis=-1)
    return x

_drawn_inputs = setup_inputs


def setup_inputs(seed=0):
    import zlib

    import numpy as np

    out = dict(_drawn_inputs(seed))
    spreads = {'L0_ffn_br': (0.0, 0.1),
     'L0_ffn_b1': (0.0, 0.1),
     'L0_ffn_b2': (0.0, 0.1),
     'L0_ffn_gamma': (1.0, 0.2),
     'L0_ffn_beta': (0.0, 0.1)}
    factors = {'L0_attn_b_out': 3.32, 'L0_attn_mask_logits': 23.25}
    for name, (base, spread) in spreads.items():
        noise = np.random.default_rng([zlib.crc32(name.encode()), seed]).standard_normal(out[name].shape)
        drawn = base * np.exp(spread * noise) if base else spread * noise
        out[name] = jnp.asarray(drawn.astype(out[name].dtype))
    for name, factor in factors.items():
        out[name] = (out[name] * factor).astype(out[name].dtype)
    return out
```

```python
from contextlib import ExitStack

import numpy as np

import concourse.bass as bass
from concourse import mybir
from concourse.alu_op_type import AluOpType as ALU

ACT = mybir.ActivationFunctionType
F32 = mybir.dt.float32
F32R = mybir.dt.float32r
I32 = mybir.dt.int32
X = mybir.AxisListType.X

NB = 8
S = 512
D = 128
H = 16
E = 8
SCALE = 1.0 / np.sqrt(8.0)
EPS = 1e-5
MAGIC = 0x5F3759DF

HS = 32
T_XIN = -16
T_Q, T_K = -10, -9
T_V = 24
T_MX = 33
T_ST = 36
T_XR = 60
T_NORM = 71
T_OUT = 72
T_X1T = 76
T_LOG = 77
T_WT = 80
T_B2 = 81
T_H = 78
T_FIN = T_H + 36
T_FIN2 = T_FIN + 3


class Counter:

    def __init__(self, sem):
        self.sem, self.n = sem, 0

    def mark(self, instruction):
        self.n += 1
        instruction.then_inc(self.sem, 1)
        return (self.sem, self.n)


class Dmas:

    def __init__(self, sem):
        self.sem, self.n = sem, 0

    def mark(self, instruction):
        self.n += 16
        instruction.then_inc(self.sem, 16)
        return (self.sem, self.n)


def build_program(nc, x, xT, wqkvT, wv, w_out, b_out, mlog, wrT, br, w1T, b1T, w2T, b2, gamma, beta,
                  basis, ident_c, desc_c, out):
    with ExitStack() as ctx:
        def sb(name, shape, dt=F32):
            return ctx.enter_context(nc.sbuf_tensor(name, shape, dt))

        def psum(name):
            return ctx.enter_context(nc.psum_tensor(name, [128, 512], F32))

        def sem(name):
            return ctx.enter_context(nc.semaphore(name))

        pe, act, dve, pool, sp = nc.tensor, nc.scalar, nc.vector, nc.gpsimd, nc.sync
        cp, ca, cv, cg = (Counter(sem(n)) for n in ("c_pe", "c_act", "c_dve", "c_pool"))
        d_w = [Dmas(sem(f"d_w{i}")) for i in range(6)]
        d_x = [Dmas(sem(f"d_x{i}")) for i in range(2)]
        d_xr = [Dmas(sem(f"d_xr{i}")) for i in range(2)]
        d_qw = [Dmas(sem(f"d_qw{i}")) for i in range(2)]
        d_qr = [Dmas(sem(f"d_qr{i}")) for i in range(2)]
        d_mw = [Dmas(sem(f"d_mw{i}")) for i in range(2)]
        d_mr = [Dmas(sem(f"d_mr{i}")) for i in range(2)]
        d_o = [Dmas(sem(f"d_o{i}")) for i in range(2)]
        d_out = [Dmas(sem(f"d_out{i}")) for i in range(2)]

        seen = {}

        def need(engine, token):
            key = (id(engine), id(token[0]))
            if seen.get(key, 0) < token[1]:
                engine.wait_ge(token[0], token[1])
                seen[key] = token[1]

        psS = [psum(f"psS{i}") for i in range(2)]
        psT = [psum(f"psT{i}") for i in range(2)]
        psO, psH, psY, psM = psum("psO"), psum("psH"), psum("psY"), psum("psM")

        ident = sb("ident", [128, 128])
        desc = sb("desc", [128, 32])
        w1h = sb("w1h", [128, 4096], F32R)
        w1l = sb("w1l", [128, 4096], F32R)
        w2s = sb("w2s", [128, 32, 128])
        QK = [sb(f"QK{i}", [128, 2, 2048], F32R) for i in range(3)]
        P = sb("P", [128, 8, 512])
        hT = sb("hT", [128, 8, 512])
        Oe = sb("Oe", [128, 4, 512])
        Oc, Dc, On = (sb(n, [128, 512]) for n in ("Oc", "Dc", "On"))
        V = [sb(f"V{i}", [128, 4, 16, 32]) for i in range(2)]
        xTs = [sb(f"xTs{i}", [128, 512]) for i in range(2)]
        xr = sb("xr", [128, 4, 128])
        qh = sb("qh", [128, 2, 512], F32R)
        ql = sb("ql", [128, 2, 512], F32R)
        mx = [sb(f"mx{i}", [128, 4, 16]) for i in range(2)]
        mh = sb("mh", [16, 2, 512], F32R)
        x1 = [sb(f"x1{i}", [128, 4, 128]) for i in range(2)]
        acc = [sb(f"acc{i}", [128, 4, 128]) for i in range(2)]
        x1T = sb("x1T", [128, 512])
        x1h = [sb(f"x1h{i}", [128, 512], F32R) for i in range(2)]
        x1l = [sb(f"x1l{i}", [128, 512], F32R) for i in range(2)]
        fin = sb("fin", [128, 4, 128])
        wrs = sb("wrs", [128, 8])
        wqk_t, cm = Oc[:, 0:256], Oc[:, 256:384]
        wqk = sb("wqk", [128, 2, 128])
        wvs = sb("wvs", [128, 128])
        wos = sb("wos", [128, 128])
        bs = Oe[:, 0:2, :].rearrange("p a b -> p (a b)")
        ml = sb("ml", [128, 8])
        b1s = sb("b1s", [128, 32])
        b2s = sb("b2s", [8, 128])
        bo, ga, be = (sb(n, [128, 128]) for n in ("bo", "ga", "be"))
        brs = sb("brs", [128, 8])
        st = sb("st", [128, 4, 6])
        mv = [sb(f"mv{i}", [128, 4, 2]) for i in range(2)]
        ve = sb("ve", [128, 4])
        rs = sb("rs", [128, 4])
        nt = sb("nt", [128, 4])
        lg, e1, t1, oh1, l2, oh2 = (sb(n, [128, 4, 8]) for n in ("lg", "e1", "t1", "oh1", "l2", "oh2"))
        rm = sb("rm", [128, 8, 4])
        wt = [sb(f"wt{i}", [128, 4, 8]) for i in range(2)]
        wTs = sb("wTs", [8, 512])

        qk_dram = [nc.dram_tensor(f"qk_dram{i}", (2, 2, 4, 8, 2048), F32, kind="Internal").ap() for i in range(2)]
        m_dram = [nc.dram_tensor(f"m_dram{i}", (16, 2, 512), F32, kind="Internal").ap() for i in range(2)]

        xr_v = x.rearrange("b (t p) d -> b p t d", p=128)
        out_v = out.rearrange("b (t p) d -> b p t d", p=128)

        def rows(ap_row, n=128):
            return ap_row.partition_broadcast(n)

        T = {}

        def load(i, dst, src):
            T["w", i] = d_w[i].mark(sp.dma_start(dst, src))

        load(0, bs[:, 0:640], basis)
        load(0, wqk_t, wqkvT)
        load(0, ml[:, 0:5], rows(mlog))
        load(1, wvs[:], wv)
        T["x", 0] = d_x[0].mark(sp.dma_start(xTs[0][:], xT[:, 0:512]))
        load(1, ident[:], ident_c)
        load(2, wos[:], w_out)
        load(2, bo[:], rows(b_out))
        load(3, hT[:].rearrange("p a b -> p (a b)"), w1T)
        load(4, w2s[:].rearrange("p a b -> p (a b)"), w2T)
        load(5, wrs[:], wrT)
        load(5, brs[:], rows(br))
        load(5, b1s[:], b1T)
        load(5, b2s[:], b2)
        load(5, ga[:], rows(gamma))
        load(5, be[:], rows(beta))
        load(5, desc[:], desc_c)

        for i in range(3):
            T["qk1", i] = cg.mark(pool.memset(QK[i][:].bitcast(F32), 1.0))
        for i in range(2):
            cg.mark(pool.memset(V[i][:], 0.0))
            need(pool, (cg.sem, cg.n))
            T["v1", i] = cg.mark(pool.memset(V[i][:, :, :, 8:16], 1.0))

        need(act, T["w", 0])
        T["sig"] = ca.mark(act.activation(ml[:, 0:5], ml[:, 0:5], ACT.Exp, scale=-1.0))
        need(dve, T["sig"])
        a = cv.mark(dve.tensor_scalar(ml[:, 0:5], ml[:, 0:5], 1.0, None, ALU.add))
        need(dve, a)
        a = cv.mark(dve.reciprocal(ml[:, 0:5], ml[:, 0:5]))
        need(dve, a)
        need(dve, T["w", 0])
        a = cv.mark(dve.tensor_scalar(cm, bs[:, 0:128], ml[:, 0:1], None, ALU.mult))
        for f in range(1, 5):
            need(dve, a)
            a = cv.mark(dve.scalar_tensor_tensor(out=cm, in0=bs[:, 128 * f:128 * f + 128], scalar=ml[:, f:f + 1],
                                                 in1=cm, op0=ALU.mult, op1=ALU.add))
        T["cm"] = a
        need(pe, T["cm"])
        for i in range(2):
            mm = pe.matmul(psM[:, 128 * i:128 * i + 128], wqk_t[:, 128 * i:128 * i + 128], cm, start=True, stop=True)
        T["fold"] = cp.mark(mm)
        need(act, T["fold"])
        ca.mark(act.mul(wqk[:, 0, :], psM[:, 0:128], float(SCALE)))
        T["wqk"] = ca.mark(act.copy(wqk[:, 1, :], psM[:, 128:256]))
        T["M"] = T["wqk"]

        def split_w1():
            need(dve, T["w", 3])
            a = None
            for i in range(8):
                w = hT[:, i, :]
                a = cv.mark(dve.tensor_copy(w1h[:, 512 * i:512 * i + 512], w))
                need(dve, a)
                a = cv.mark(dve.tensor_tensor(w1l[:, 512 * i:512 * i + 512], w, w1h[:, 512 * i:512 * i + 512],
                                              ALU.subtract))
            T["w1"] = a

        def x_in(b):
            i = b % 2
            if b >= 2:
                need(sp, T["v_pe", b - 2])
            if b > 0:
                T["x", b] = d_x[i].mark(sp.dma_start(xTs[i][:], xT[:, 512 * b:512 * b + 512]))

        def residual_in(b):
            if b >= 1:
                need(sp, T["r1", b - 1])
            T["xr", b] = d_xr[b % 2].mark(sp.dma_start(xr[:], xr_v[b]))

        def m_free():
            need(pe, T["M"])

        def project(b, w):
            need(pe, T["x", b])
            need(pe, T["wqk"])
            m_free()
            T["q_pe", b, w] = cp.mark(pe.matmul(psM[:], wqk[:, w, :], xTs[b % 2][:], start=True, stop=True))
            need(dve, T["q_pe", b, w])
            if b > 0:
                need(dve, T["qw", b - 1])
            T["q_h", b, w] = cv.mark(dve.tensor_copy(qh[:, w, :], psM[:]))
            need(dve, T["q_h", b, w])
            T["q_l", b, w] = cv.mark(dve.tensor_tensor(ql[:, w, :], psM[:], qh[:, w, :], ALU.subtract))
            T["M"] = T["q_l", b, w]

        def spread(b):
            i = b % 2
            tile = QK[b % 3]
            dr = qk_dram[i]
            need(sp, T["q_l", b, 1])
            if b >= 2:
                need(sp, T["qr", b - 2])
            for n, s in enumerate((qh, ql)):
                for w in range(2):
                    T["qw", b] = d_qw[i].mark(sp.dma_start(
                        dr[n, w].rearrange("j d (g q) -> (j d g) q", g=4), s[:, w, :].bitcast(F32)))
            need(sp, T["qw", b])
            need(sp, T["qk1", b % 3])
            if b >= 3:
                need(sp, T["st_pe", b - 3, 15, 1])
            for j in range(4):
                p = 32 * j
                T["qr", b] = d_qr[i].mark(sp.dma_start(
                    tile[p:p + 8, :, :].bitcast(F32), dr[0, :, j].rearrange("w d q -> d w q")))
                for r, w, n in ((8, 0, 0), (8, 1, 1), (16, 0, 1), (16, 1, 0)):
                    T["qr", b] = d_qr[i].mark(sp.dma_start(tile[p + r:p + r + 8, w, :].bitcast(F32), dr[n, w, j]))

        def values(b):
            i = b % 2
            need(pe, T["w", 1])
            m_free()
            for t in range(4):
                mm = pe.matmul(psM[:, 128 * t:128 * t + 128], xTs[i][:, 128 * t:128 * t + 128], wvs[:],
                               start=True, stop=True)
            T["v_pe", b] = cp.mark(mm)
            need(act, T["v_pe", b])
            need(act, T["v1", i])
            if b >= 2:
                need(act, T["pv_pe", b - 2, 3])
            T["v", b] = ca.mark(act.copy(V[i][:, :, :, 0:8], psM[:].rearrange("p (t h d) -> p t h d", t=4, h=16)))
            T["M"] = T["v", b]

        def s_pair(b, slot, p):
            g, t = divmod(slot, 4)
            tile = QK[b % 3]
            need(pe, T["qr", b])
            for j in (2 * p, 2 * p + 1):
                k = j % 2
                if ("smax", k) in T:
                    need(pe, T["smax", k])
                q0 = 512 * g + 128 * t
                T["s_pe", k] = cp.mark(pe.matmul(psS[k][:], tile[32 * j:32 * j + 24, 0, q0:q0 + 128],
                                                 tile[32 * j:32 * j + 24, 1, 512 * g:512 * g + 512],
                                                 start=True, stop=True))

        def max_pair(b, slot, p):
            g, t = divmod(slot, 4)
            for j in (2 * p, 2 * p + 1):
                k = j % 2
                need(dve, T["s_pe", k])
                if b >= 2 and slot == 0:
                    need(dve, T["mx_pe", b - 2])
                c = 4 * j + g
                T["smax", k] = cv.mark(dve.tensor_reduce(mx[b % 2][:, t, c:c + 1], psS[k][:], X, ALU.max))
                T["max", b] = T["smax", k]

        def maxima(b):
            i = b % 2
            need(pe, T["max", b])
            need(pe, T["w", 1])
            m_free()
            for t in range(4):
                mm = pe.transpose(psM[0:16, 128 * t:128 * t + 128], mx[i][:, t, :], ident[:])
            T["mx_pe", b] = cp.mark(mm)
            need(dve, T["mx_pe", b])
            if b > 0:
                need(dve, T["mw", b - 1])
            a = cv.mark(dve.tensor_scalar(mh[:, 0, :], psM[0:16, :], -1.0, None, ALU.mult))
            need(dve, a)
            T["mh", b] = cv.mark(dve.scalar_tensor_tensor(out=mh[:, 1, :], in0=psM[0:16, :], scalar=-1.0,
                                                          in1=mh[:, 0, :], op0=ALU.mult, op1=ALU.subtract))
            T["M"] = T["mh", b]
            need(sp, T["mh", b])
            if b >= 2:
                need(sp, T["mr", b - 2])
            T["mw", b] = d_mw[i].mark(sp.dma_start(m_dram[i], mh[:].bitcast(F32)))
            need(sp, T["mw", b])
            md = m_dram[i].rearrange("(j g) n q -> n j g q", g=4)
            for n in range(2):
                T["mr", b] = d_mr[i].mark(sp.dma_start(
                    QK[b % 3][24 + n:128:32, 0, :].rearrange("p (g q) -> p g q", g=4).bitcast(F32), md[n]))

        def st_pair(b, slot, p):
            g, kt = divmod(slot, 4)
            tile = QK[b % 3]
            need(pe, T["mr", b])
            for j in (2 * p, 2 * p + 1):
                k = j % 2
                if ("exp", k) in T:
                    need(pe, T["exp", k])
                k0 = 512 * g + 128 * kt
                T["t_pe", k] = cp.mark(pe.matmul(psT[k][:], tile[32 * j:32 * j + 26, 1, k0:k0 + 128],
                                                 tile[32 * j:32 * j + 26, 0, 512 * g:512 * g + 512],
                                                 start=True, stop=True))
            T["st_pe", b, slot, p] = T["t_pe", 1]

        def exp_pair(b, slot, p):
            for j in (2 * p, 2 * p + 1):
                k = j % 2
                need(act, T["t_pe", k])
                ring = (slot * 4 + j) % 8
                if ("pring", ring) in T:
                    need(act, T["pring", ring])
                T["exp", k] = ca.mark(act.activation(P[:, ring, :], psT[k][:], ACT.Exp))
                T["p", b, slot, j] = (T["exp", k], ring)

        def weighted(b, slot):
            g, kt = divmod(slot, 4)
            need(pe, T["v", b])
            if kt == 0 and "oe" in T:
                need(pe, T["oe"])
            for j in range(4):
                tok, ring = T["p", b, slot, j]
                need(pe, tok)
                mm = pe.matmul(psO[32 * j:32 * j + 32, :], V[b % 2][:, kt, 4 * g + j, :], P[:, ring, :],
                               start=kt == 0, stop=kt == 3)
            tok = cp.mark(mm)
            for j in range(4):
                T["pring", T["p", b, slot, j][1]] = tok
            if kt == 3:
                T["pv_pe", b, g] = tok
                need(act, tok)
                if b > 0:
                    need(act, T["oc", b - 1])
                T["oe"] = ca.mark(act.copy(Oe[:, g, :], psO[:]))
                need(sp, T["oe"])
                if b > 0 and g == 0:
                    need(sp, T["norm", b - 1])
                for j in range(4):
                    r = 32 * g + 8 * j
                    d_o[b % 2].mark(sp.dma_start(Oc[r:r + 8, :], Oe[32 * j:32 * j + 8, g, :]))
                    T["oc", b] = d_o[b % 2].mark(sp.dma_start(Dc[r:r + 8, :], Oe[32 * j + 8:32 * j + 16, g, :]))

        def normalise(b):
            need(dve, T["oc", b])
            a = cv.mark(dve.reciprocal(Dc[:], Dc[:]))
            need(dve, a)
            if b > 0:
                need(dve, T["out_pe", b - 1])
            T["norm", b] = cv.mark(dve.tensor_tensor(On[:], Oc[:], Dc[:], ALU.mult))
            i = b % 2
            need(pool, T["xr", b])
            need(pool, T["w", 2])
            T["xb", b] = cg.mark(pool.tensor_tensor(xr[:], xr[:],
                                                    bo[:].unsqueeze(1).to_broadcast([128, 4, 128]), ALU.add))

        def rstd(mean_var):
            a = cg.mark(pool.tensor_scalar(ve[:], mean_var[:, :, 1], EPS, 0.0, ALU.add, ALU.add))
            need(dve, a)
            a = cv.mark(dve.tensor_scalar(rs[:].bitcast(I32), ve[:].bitcast(I32), 1, None, ALU.logical_shift_right))
            need(dve, a)
            a = cv.mark(dve.tensor_scalar(rs[:].bitcast(I32), rs[:].bitcast(I32), -1, MAGIC, ALU.mult, ALU.add))
            need(pool, a)
            for _ in range(3):
                a = cg.mark(pool.tensor_tensor(nt[:], rs[:], rs[:], ALU.mult))
                need(pool, a)
                a = cg.mark(pool.tensor_tensor(nt[:], nt[:], ve[:], ALU.mult))
                need(pool, a)
                a = cg.mark(pool.tensor_scalar(nt[:], nt[:], -0.5, 1.5, ALU.mult, ALU.add))
                need(pool, a)
                a = cg.mark(pool.tensor_tensor(rs[:], rs[:], nt[:], ALU.mult))
                need(pool, a)
            return a

        def statistics(src, mean_var, before):
            for tok in before:
                need(dve, tok)
            for t in range(4):
                a = cv.mark(dve.bn_stats(st[:, t, :], src[:, t, :]))
            need(dve, a)
            for t in range(4):
                a = cv.mark(dve.bn_aggr(mean_var[:, t, :], st[:, t, :]))
            need(pool, a)
            return rstd(mean_var)

        def shifted(engine, counter, dst, src, mean_var):
            for t in range(4):
                a = counter.mark(engine.tensor_scalar(dst[:, t, :], src[:, t, :], mean_var[:, t, 0:1], rs[:, t:t + 1],
                                                      ALU.subtract, ALU.mult))
            return a

        def project_out(b):
            i = b % 2
            need(pe, T["norm", b])
            need(pe, T["w", 2])
            m_free()
            for t in range(4):
                mm = pe.matmul(psM[:, 128 * t:128 * t + 128], On[:, 128 * t:128 * t + 128], wos[:],
                               start=True, stop=True)
            T["out_pe", b] = cp.mark(mm)
            need(dve, T["out_pe", b])
            need(dve, T["xb", b])
            if b >= 2:
                need(dve, T["fin_dve", b - 2])
            if b >= 1:
                need(dve, T["lnapply"])
            T["r1", b] = cv.mark(dve.tensor_tensor(acc[i][:], psM[:].rearrange("p (t d) -> p t d", t=4), xr[:],
                                                   ALU.add))
            T["M"] = T["r1", b]
            if b >= 2:
                need(pool, T["x1_last", b - 2])
            statistics(acc[i], mv[0], [T["r1", b]])
            T["x1", b] = shifted(pool, cg, x1[i], acc[i], mv[0])
            T["lnapply"] = T["x1", b]

        def turn_x1(b):
            i = b % 2
            need(pe, T["x1", b])
            m_free()
            for t in range(4):
                mm = pe.transpose(psM[:, 128 * t:128 * t + 128], x1[i][:, t, :], ident[:])
            T["x1_pe", b] = cp.mark(mm)
            need(dve, T["x1_pe", b])
            if b >= 2:
                need(dve, T["h_pe", b - 2])
            a = cv.mark(dve.tensor_copy(x1h[i][:], psM[:]))
            need(dve, a)
            T["x1l", b] = cv.mark(dve.tensor_tensor(x1l[i][:], psM[:], x1h[i][:], ALU.subtract))
            if b >= 1:
                need(dve, T["log_pe", b - 1])
            T["x1T", b] = cv.mark(dve.tensor_copy(x1T[:], psM[:]))
            T["M"] = T["x1T", b]

        def route(b):
            i = b % 2
            need(pe, T["x1T", b])
            need(pe, T["w", 5])
            m_free()
            for t in range(4):
                mm = pe.matmul(psM[:, 8 * t:8 * t + 8], x1T[:, 128 * t:128 * t + 128], wrs[:], start=True, stop=True)
            T["log_pe", b] = cp.mark(mm)
            need(dve, T["log_pe", b])
            need(dve, T["w", 5])

            def over(ap):
                return ap.unsqueeze(2).to_broadcast([128, 4, 8])

            def do(ins):
                a = cv.mark(ins)
                need(dve, a)
                return a

            dsc = desc[:].rearrange("p (t e) -> p t e", t=4)
            T["M"] = do(dve.tensor_tensor(lg[:], psM[:, 0:32].rearrange("p (t e) -> p t e", t=4),
                                          brs[:].unsqueeze(1).to_broadcast([128, 4, 8]), ALU.add))
            for n, (l, oh) in enumerate(((lg, oh1), (l2, oh2))):
                do(dve.tensor_reduce(rm[:, 2 * n, :], l[:], X, ALU.max))
                do(dve.tensor_tensor(e1[:], l[:], over(rm[:, 2 * n, :]), ALU.is_ge))
                do(dve.tensor_tensor(t1[:], e1[:], dsc, ALU.mult))
                do(dve.tensor_reduce(rm[:, 2 * n + 1, :], t1[:], X, ALU.max))
                do(dve.tensor_tensor(oh[:], t1[:], over(rm[:, 2 * n + 1, :]), ALU.is_equal))
                if n == 0:
                    do(dve.scalar_tensor_tensor(out=l2[:], in0=oh1[:], scalar=-3e38, in1=lg[:],
                                                op0=ALU.mult, op1=ALU.add))
            T["gap", b] = do(dve.tensor_tensor(rm[:, 4, :], rm[:, 2, :], rm[:, 0, :], ALU.subtract))
            need(act, T["gap", b])
            T["gexp", b] = ca.mark(act.activation(rm[:, 5, :], rm[:, 4, :], ACT.Exp))

        def route2(b):
            i = b % 2

            def over(ap):
                return ap.unsqueeze(2).to_broadcast([128, 4, 8])

            def do(ins):
                a = cv.mark(ins)
                need(dve, a)
                return a

            need(dve, T["gexp", b])
            do(dve.tensor_scalar(rm[:, 6, :], rm[:, 5, :], 1.0, None, ALU.add))
            do(dve.reciprocal(rm[:, 6, :], rm[:, 6, :]))
            do(dve.tensor_tensor(rm[:, 7, :], rm[:, 5, :], rm[:, 6, :], ALU.mult))
            do(dve.tensor_tensor(oh1[:], oh1[:], over(rm[:, 6, :]), ALU.mult))
            do(dve.tensor_tensor(oh2[:], oh2[:], over(rm[:, 7, :]), ALU.mult))
            T["wt", b] = do(dve.tensor_tensor(wt[i][:], oh1[:], oh2[:], ALU.add))

        def turn_w(b):
            i = b % 2
            need(pe, T["wt", b])
            m_free()
            for t in range(4):
                mm = pe.transpose(psM[0:8, 128 * t:128 * t + 128], wt[i][:, t, :], ident[:])
            T["wT_pe", b] = cp.mark(mm)
            need(act, T["wT_pe", b])
            if b > 0:
                need(act, T["b2_pe", b - 1])
            T["wT", b] = ca.mark(act.copy(wTs[:], psM[0:8, :]))
            T["M"] = T["wT", b]

        def bias2(b):
            i = b % 2
            need(pe, T["wT", b])
            m_free()
            for t in range(4):
                mm = pe.matmul(psM[:, 128 * t:128 * t + 128], wTs[:, 128 * t:128 * t + 128], b2s[:],
                               start=True, stop=True)
            T["b2_pe", b] = cp.mark(mm)
            need(dve, T["b2_pe", b])
            need(dve, T["x1", b])
            T["acc", b] = cv.mark(dve.tensor_tensor(acc[i][:], psM[:].rearrange("p (t d) -> p t d", t=4), x1[i][:],
                                                    ALU.add))
            T["M"] = T["acc", b]
            need(pool, T["acc", b])
            need(pool, T["x1_pe", b])
            T["x1b", b] = cg.mark(pool.tensor_tensor(x1[i][:], x1[i][:],
                                                     be[:].unsqueeze(1).to_broadcast([128, 4, 128]), ALU.add))

        def hidden(b, m):
            i = b % 2
            need(pe, T["x1l", b])
            need(pe, T["w1"])
            if "relu" in T:
                need(pe, T["relu"])
            c = 128 * m
            pe.matmul(psH[:], w1h[:, c:c + 128], x1l[i][:], start=True, stop=False)
            pe.matmul(psH[:], w1l[:, c:c + 128], x1h[i][:], start=False, stop=False)
            T["h_pe", b] = cp.mark(pe.matmul(psH[:], w1h[:, c:c + 128], x1h[i][:], start=False, stop=True))
            need(act, T["h_pe", b])
            if ("hring", m % 8) in T:
                need(act, T["hring", m % 8])
            T["relu"] = ca.mark(act.activation(hT[:, m % 8, :], psH[:], ACT.Relu, bias=b1s[:, m:m + 1]))
            T["h", b, m] = T["relu"]

        def experts(b, e, part):
            need(pe, T["w", 4])
            lo, hi = ((0, 6), (6, 11), (11, 16))[part]
            if part == 0:
                need(pe, T["h", b, 4 * e + 3])
                if "yacc" in T:
                    need(pe, T["yacc"])
            for n in range(lo, hi):
                t, f = divmod(n, 4)
                mm = pe.matmul(psY[:, 128 * t:128 * t + 128], hT[:, (4 * e + f) % 8, 128 * t:128 * t + 128],
                               w2s[:, 4 * e + f, :], start=f == 0, stop=f == 3)
            if part == 2:
                T["y_pe", b, e] = cp.mark(mm)
                for f in range(4):
                    T["hring", (4 * e + f) % 8] = T["y_pe", b, e]

        def gather(b, e):
            i = b % 2
            need(dve, T["y_pe", b, e])
            need(dve, T["acc", b] if e == 0 else T["yacc"])
            for t in range(4):
                a = cv.mark(dve.scalar_tensor_tensor(out=acc[i][:, t, :], in0=psY[:, 128 * t:128 * t + 128],
                                                     scalar=wt[i][:, t, e:e + 1], in1=acc[i][:, t, :],
                                                     op0=ALU.mult, op1=ALU.add))
            T["yacc"] = a
            T["yl", b] = a

        def finish(b):
            i = b % 2
            need(pool, T["lnapply"])
            statistics(acc[i], mv[1], [T["yl", b], T["lnapply"]])
            a = shifted(pool, cg, fin, acc[i], mv[1]) if b == 0 else None
            if b > 0:
                need(pool, T["out", b - 1])
                a = shifted(pool, cg, fin, acc[i], mv[1])
            T["lnapply"] = a
            need(pool, a)
            a = cg.mark(pool.tensor_tensor(fin[:], fin[:], ga[:].unsqueeze(1).to_broadcast([128, 4, 128]), ALU.mult))
            need(pool, a)
            T["fin", b] = cg.mark(pool.tensor_tensor(fin[:], fin[:], x1[i][:], ALU.add))
            T["x1_last", b] = T["fin", b]

        def finish2(b):
            i = b % 2
            T["fin_dve", b] = T["fin", b]
            statistics(fin, mv[1], [T["fin", b], T["lnapply"]])
            T["lnapply"] = shifted(pool, cg, fin, fin, mv[1])
            need(sp, T["lnapply"])
            T["out", b] = d_out[i].mark(sp.dma_start(out_v[b], fin[:]))

        need(pe, T["w", 1])
        for G in range(-16, HS * (NB - 1) + T_FIN2 + 1):
            for b in range(NB):
                s = G - HS * b
                if s == T_XIN:
                    x_in(b)
                if s == T_Q:
                    project(b, 0)
                if s == T_K:
                    project(b, 1)
                    spread(b)
            if G == -4:
                split_w1()
            for b in range(NB):
                s = G - HS * b
                if T_ST <= s < T_ST + 32:
                    st_pair(b, (s - T_ST) // 2, (s - T_ST) % 2)
                    exp_pair(b, (s - T_ST) // 2, (s - T_ST) % 2)
            for b in range(NB):
                s = G - HS * b
                if T_ST + 2 <= s < T_ST + 34 and (s - T_ST) % 2 == 0:
                    weighted(b, (s - T_ST - 2) // 2)
            for b in range(NB):
                m = G - HS * b - T_H
                if 0 <= m < 32:
                    hidden(b, m)
            for b in range(NB):
                s = G - HS * b
                if 0 <= s < 32:
                    s_pair(b, s // 2, s % 2)
                    max_pair(b, s // 2, s % 2)
            for b in range(NB):
                m = G - HS * b - T_H - 4
                if 0 <= m < 32:
                    e, r = divmod(m, 4)
                    if r < 3:
                        experts(b, e, r)
                    else:
                        gather(b, e)
            for b in range(NB):
                s = G - HS * b
                for at, do in ((T_V, values), (T_XR, residual_in), (T_MX, maxima), (T_NORM, normalise), (T_OUT, project_out),
                               (T_X1T, turn_x1), (T_LOG, route), (T_LOG + 1, route2), (T_WT, turn_w), (T_B2, bias2),
                               (T_FIN, finish), (T_FIN2, finish2)):
                    if s == at:
                        do(b)
        for b in range(NB - 2, NB):
            need(sp, T["out", b])
            need(sp, T["qw", b])
            need(sp, T["mw", b])


def _constants():
    n = np.arange(8)
    k = (n[:, None] - n[None, :]) % 8
    basis = np.zeros((128, 5, 128), np.float32)
    for f in range(5):
        c = np.cos(2 * np.pi * f * k / 8) / 8 * (1 if f in (0, 4) else 2)
        for g in range(4):
            for j in range(4):
                h = 4 * g + j
                for a in range(8):
                    for d in range(8):
                        basis[8 * h + a, f, 32 * j + 4 * d + g] = c[a, d]
    desc = np.tile(np.arange(8, 0, -1, dtype=np.float32), (128, 4))
    return basis.reshape(128, 640), np.eye(128, dtype=np.float32), np.ascontiguousarray(desc)


def kernel(**inputs):
    import concourse.bacc as bacc
    from concourse.bass_utils import run_bass_kernel_spmd

    a = {k: np.asarray(v) for k, v in inputs.items()}
    x = a["L0_attn_x"]
    wqkv = a["L0_attn_w_qkv"]
    W1, W2, b1 = a["L0_ffn_W1"], a["L0_ffn_W2"], a["L0_ffn_b1"]
    basis, ident, desc = _constants()
    arrays = {
        "x": x,
        "xT": x.reshape(4096, 128).T,
        "wqkvT": np.concatenate([wqkv[:, 0:128].T, wqkv[:, 128:256].T], axis=1),
        "wv": wqkv[:, 256:384],
        "w_out": a["L0_attn_w_out"],
        "b_out": a["L0_attn_b_out"],
        "mlog": a["L0_attn_mask_logits"],
        "wrT": a["L0_ffn_Wr"].T,
        "br": a["L0_ffn_br"],
        "w1T": W1.reshape(4096, 128).T,
        "b1T": b1.reshape(32, 128).T,
        "w2T": W2.transpose(0, 2, 1).reshape(32, 128, 128).transpose(1, 0, 2).reshape(128, 4096),
        "b2": a["L0_ffn_b2"],
        "gamma": a["L0_ffn_gamma"],
        "beta": a["L0_ffn_beta"],
        "basis": basis, "ident_c": ident, "desc_c": desc,
    }
    arrays = {f"in_{k}": np.ascontiguousarray(v) for k, v in arrays.items()}
    nc = bacc.Bacc("TRN2", target_bir_lowering=False, num_devices=1)
    args = [nc.dram_tensor(n, v.shape, mybir.dt.from_np(v.dtype), kind="ExternalInput").ap() for n, v in arrays.items()]
    args.append(nc.dram_tensor("out_dram", (8, 512, 128), F32, kind="ExternalOutput").ap())
    build_program(nc, *args)
    r = run_bass_kernel_spmd(nc, [arrays], core_ids=[0])
    return r.results[0]["out_dram"]
```

```python
from contextlib import ExitStack

import numpy as np

import concourse.bass as bass
from concourse import mybir
from concourse.alu_op_type import AluOpType as ALU

ACT = mybir.ActivationFunctionType
F32 = mybir.dt.float32
F32R = mybir.dt.float32r
I32 = mybir.dt.int32
X = mybir.AxisListType.X

NB = 8
S = 512
D = 128
H = 16
E = 8
SCALE = 1.0 / np.sqrt(8.0)
EPS = 1e-5
MAGIC = 0x5F3759DF

HS = 32
T_XIN = -16
T_Q, T_K = -12, -11
T_HALF = 7
T_V = 24
T_MX = 32
T_ST = 37
T_XR = 60
T_CHAIN = T_ST + 37
T_H = T_CHAIN + 12
BURST, D1, D2 = 34, 3, 3
DUMMY = {G: BURST if G < 0 else D1 if G < T_ST else D2 for G in range(-1, T_H)}
LAG = 3
M_FIN = LAG + 33
Y_OUT, Y_X1, Y_ROUTE, Y_WT = 4, 3, 2, 3


class Counter:

    def __init__(self, sem):
        self.sem, self.n = sem, 0

    def mark(self, instruction):
        self.n += 1
        instruction.then_inc(self.sem, 1)
        return (self.sem, self.n)


class Dmas:

    def __init__(self, sem):
        self.sem, self.n = sem, 0

    def mark(self, instruction):
        self.n += 16
        instruction.then_inc(self.sem, 16)
        return (self.sem, self.n)


def build_program(nc, x, xT, wqkvT, wv, w_out, b_out, mlog, wrT, br, w1T, b1T, w2T, b2T, gamma, beta,
                  basis, ident_c, desc_c, out):
    with ExitStack() as ctx:
        def sb(name, shape, dt=F32):
            return ctx.enter_context(nc.sbuf_tensor(name, shape, dt))

        def psum(name):
            return ctx.enter_context(nc.psum_tensor(name, [128, 512], F32))

        def sem(name):
            return ctx.enter_context(nc.semaphore(name))

        pe, act, dve, pool, sp = nc.tensor, nc.scalar, nc.vector, nc.gpsimd, nc.sync
        cp, ca, cv, cg = (Counter(sem(n)) for n in ("c_pe", "c_act", "c_dve", "c_pool"))
        d_w = [Dmas(sem(f"d_w{i}")) for i in range(8)]
        d_x, d_xr, d_qw, d_q0, d_q1, d_mw, d_mr, d_o, d_ww, d_out = (
            [Dmas(sem(f"d_{n}{i}")) for i in range(2)]
            for n in ("x", "xr", "qw", "q0", "q1", "mw", "mr", "o", "ww", "out"))
        d_wb = [Dmas(sem(f"d_wb{i}")) for i in range(3)]

        seen = {}

        def need(engine, token):
            key = (id(engine), id(token[0]))
            if seen.get(key, 0) < token[1]:
                engine.wait_ge(token[0], token[1])
                seen[key] = token[1]

        psS = [psum(f"psS{i}") for i in range(2)]
        psT = [psum(f"psT{i}") for i in range(2)]
        psO, psH, psY, psM = psum("psO"), psum("psH"), psum("psY"), psum("psM")

        ident = sb("ident", [128, 128])
        desc = sb("desc", [128, 32])
        w1h, w1l, w2h, w2l = (sb(n, [128, 4096], F32R) for n in ("w1h", "w1l", "w2h", "w2l"))
        QK = [sb(f"QK{i}", [128, 2, 2048], F32R) for i in range(2)]
        P = sb("P", [128, 8, 512])
        hF = sb("hF", [128, 3, 512])
        hH = sb("hH", [128, 5, 512], F32R)
        hL = sb("hL", [128, 5, 512], F32R)
        Oe = sb("Oe", [128, 2, 512])
        Oc, Dc, On = (sb(n, [128, 512]) for n in ("Oc", "Dc", "On"))
        V = [sb(f"V{i}", [128, 4, 16, 16]) for i in range(2)]
        xTs = [sb(f"xTs{i}", [128, 512]) for i in range(2)]
        xr, R, fin = (sb(n, [128, 4, 128]) for n in ("xr", "R", "fin"))
        F = R
        qh = sb("qh", [128, 512], F32R)
        ql = sb("ql", [128, 512], F32R)
        mx = [sb(f"mx{i}", [128, 4, 16]) for i in range(2)]
        mh = sb("mh", [16, 2, 512], F32R)
        x1 = [sb(f"x1{i}", [128, 4, 128]) for i in range(2)]
        x1T = On
        x1h = [sb(f"x1h{i}", [128, 512], F32R) for i in range(2)]
        x1l = [sb(f"x1l{i}", [128, 512], F32R) for i in range(2)]
        accT = [sb(f"accT{i}", [128, 512]) for i in range(2)]
        tt = sb("tt", [128, 512])
        Wb = [sb(f"Wb{i}", [128, 512]) for i in range(3)]
        wTs = sb("wTs", [8, 512])
        wrs = sb("wrs", [128, 8])
        wqk_t, cm = Oc[:, 0:256], Oc[:, 256:384]
        wqk = sb("wqk", [128, 2, 128])
        wvs = sb("wvs", [128, 128])
        wos = sb("wos", [128, 128])
        bs = Oe[:].rearrange("p a b -> p (a b)")
        ml = sb("ml", [128, 8])
        b1s = sb("b1s", [128, 32])
        b2s = sb("b2s", [128, 8])
        bo, ga, be = (sb(n, [128, 128]) for n in ("bo", "ga", "be"))
        brs = sb("brs", [128, 8])
        lg, e1, t1, oh1, l2, oh2 = (sb(n, [128, 4, 8]) for n in ("lg", "e1", "t1", "oh1", "l2", "oh2"))
        rm = sb("rm", [128, 8, 4])
        wt = sb("wt", [128, 4, 8])
        stat = [sb(f"stat{i}", [128, 4, 6]) for i in range(3)]
        mvs = [sb(f"mvs{i}", [128, 4, 2]) for i in range(3)]
        sml = [sb(f"sml{i}", [128, 3, 4]) for i in range(3)]

        qk_dram = [nc.dram_tensor(f"qk_dram{i}", (4, 2, 3, 8, 2048), F32, kind="Internal").ap() for i in range(2)]
        m_dram = [nc.dram_tensor(f"m_dram{i}", (16, 2, 512), F32, kind="Internal").ap() for i in range(2)]
        w_dram = [nc.dram_tensor(f"w_dram{i}", (8, 512), F32, kind="Internal").ap() for i in range(2)]

        xr_v = x.rearrange("b (t p) d -> b p t d", p=128)
        out_v = out.rearrange("b (t p) d -> b p t d", p=128)

        def rows(ap_row, n=128):
            return ap_row.partition_broadcast(n)

        T = {}

        def load(i, dst, src):
            T["w", i] = d_w[i].mark(sp.dma_start(dst, src))

        load(0, bs[:, 0:640], basis)
        load(0, wqk_t, wqkvT)
        load(0, ml[:, 0:5], rows(mlog))
        T["x", 0] = d_x[0].mark(sp.dma_start(xTs[0][:], xT[:, 0:512]))
        load(1, ident[:], ident_c)
        load(1, wvs[:], wv)
        load(3, P[:].rearrange("p a b -> p (a b)"), w1T)
        load(2, wos[:], w_out)
        load(2, bo[:], rows(b_out))
        load(5, wrs[:], wrT)
        load(5, brs[:], rows(br))
        load(5, b1s[:], b1T)
        load(5, b2s[:], b2T)
        load(5, ga[:], rows(gamma))
        load(5, be[:], rows(beta))
        load(5, desc[:], desc_c)

        for i in range(2):
            T["qk1", i] = cg.mark(pool.memset(QK[i][:, 1, :].bitcast(F32), 1.0))
        for i in range(2):
            T["v1", i] = cg.mark(pool.memset(V[i][:], 1.0))
        zero = cv.mark(dve.memset(R[:], 0.0))
        need(pe, zero)
        T["o0"] = cp.mark(pe.matmul(psO[:], R[:, 0, :], R[:].rearrange("p t d -> p (t d)"), start=True, stop=True))

        need(act, T["w", 0])
        T["sig"] = ca.mark(act.activation(ml[:, 0:5], ml[:, 0:5], ACT.Exp, scale=-1.0))
        need(dve, T["sig"])
        a = cv.mark(dve.tensor_scalar(ml[:, 0:5], ml[:, 0:5], 1.0, None, ALU.add))
        need(dve, a)
        a = cv.mark(dve.reciprocal(ml[:, 0:5], ml[:, 0:5]))
        need(dve, a)
        need(dve, T["w", 0])
        a = cv.mark(dve.tensor_scalar(cm, bs[:, 0:128], ml[:, 0:1], None, ALU.mult))
        for f in range(1, 5):
            need(dve, a)
            a = cv.mark(dve.scalar_tensor_tensor(out=cm, in0=bs[:, 128 * f:128 * f + 128], scalar=ml[:, f:f + 1],
                                                 in1=cm, op0=ALU.mult, op1=ALU.add))
        T["cm"] = a
        need(pe, T["cm"])
        for i in range(2):
            mm = pe.matmul(psM[:, 128 * i:128 * i + 128], wqk_t[:, 128 * i:128 * i + 128], cm, start=True, stop=True)
        T["fold"] = cp.mark(mm)
        need(act, T["fold"])
        ca.mark(act.mul(wqk[:, 0, :], psM[:, 0:128], float(SCALE)))
        T["wqk"] = ca.mark(act.copy(wqk[:, 1, :], psM[:, 128:256]))
        T["M"] = T["wqk"]

        def split(name, hi, lo):
            for i in range(8):
                c = slice(512 * i, 512 * i + 512)
                need(act, T["w", name])
                a = ca.mark(act.copy(hi[:, c], P[:, i, :]))
                T.setdefault("w1h", a)
                need(pool, a)
                T["split", name] = cg.mark(pool.tensor_tensor(lo[:, c], P[:, i, :], hi[:, c], ALU.subtract))

        def split_second():
            need(sp, T["split", 3])
            load(4, P[:].rearrange("p a b -> p (a b)"), w2T)
            split(4, w2h, w2l)

        def x_in(b):
            if b >= 2:
                need(sp, T["v_pe", b - 2])
            if b > 0:
                T["x", b] = d_x[b % 2].mark(sp.dma_start(xTs[b % 2][:], xT[:, 512 * b:512 * b + 512]))

        def residual_in(b):
            if b >= 1:
                need(sp, T["r1", b - 1])
            T["xr", b] = d_xr[b % 2].mark(sp.dma_start(xr[:], xr_v[b]))
            need(pool, T["xr", b])
            need(pool, T["w", 2])
            T["xb", b] = cg.mark(pool.tensor_tensor(xr[:], xr[:], bo[:].unsqueeze(1).to_broadcast([128, 4, 128]),
                                                    ALU.add))

        def m_take():
            while "M" not in T:
                yield 1
            token = T.pop("M")
            yield 1
            need(pe, token)

        def project(b, w):
            yield from m_take()
            need(pe, T["x", b])
            need(pe, T["wqk"])
            T["q_pe", b, w] = cp.mark(pe.matmul(psM[:], wqk[:, w, :], xTs[b % 2][:], start=True, stop=True))
            yield 1
            need(dve, T["q_pe", b, w])
            hi, lo = (hH[:, 0, :], hL[:, 0, :]) if b == 0 and w else (qh[:], ql[:])
            if b > 0 or w == 0:
                if "qw" in T:
                    need(dve, T["qw"])
            T["q_h"] = cv.mark(dve.tensor_copy(hi, psM[:]))
            yield 1
            need(dve, T["q_h"])
            T["q_l", b, w] = cv.mark(dve.tensor_tensor(lo, psM[:], hi, ALU.subtract))
            T["M"] = T["q_l", b, w]
            need(sp, T["q_l", b, w])
            if b >= 2:
                need(sp, T["q1", b - 2])
            for r, s in ((0, hi), (1, lo if w else hi), (2, hi if w else lo)):
                T["qw"] = d_qw[b % 2].mark(sp.dma_start(
                    qk_dram[b % 2][:, w, r].rearrange("j d (g q) -> j (d g) q", g=4), s.bitcast(F32)))
            T["qw", b] = T["qw"]
            if w == 1:
                spread(b, 0)

        def spread(b, half):
            tile, dr, d = QK[b % 2], qk_dram[b % 2], (d_q0, d_q1)[half][b % 2]
            need(sp, T["qw", b])
            need(sp, T["qk1", b % 2])
            if b >= 2:
                need(sp, T["st_pe", b - 2, 8 * half + 7])
            c = slice(1024 * half, 1024 * half + 1024)
            for j in range(4):
                T["q%d" % half, b] = d.mark(sp.dma_start(
                    tile[32 * j:32 * j + 24, :, c].bitcast(F32),
                    dr[j, :, :, :, c].rearrange("w r d q -> (r d) w q")))

        def values(b):
            i = b % 2
            yield from m_take()
            need(pe, T["w", 1])
            for t in range(4):
                mm = pe.matmul(psM[:, 128 * t:128 * t + 128], xTs[i][:, 128 * t:128 * t + 128], wvs[:],
                               start=True, stop=True)
            T["v_pe", b] = cp.mark(mm)
            yield 2
            need(act, T["v_pe", b])
            need(act, T["v1", i])
            if b >= 2:
                need(act, T["pv_pe", b - 2, 3])
            T["v", b] = ca.mark(act.copy(V[i][:, :, :, 0:8], psM[:].rearrange("p (t h d) -> p t h d", t=4, h=16)))
            T["M"] = T["v", b]

        def s_bank(b, slot, p, k):
            return ("T", k, psT[k]) if b == 0 and p else ("S", k, psS[k])

        def s_pair(b, slot, p):
            g, t = divmod(slot, 4)
            tile = QK[b % 2]
            need(pe, T["q%d" % (g // 2), b])
            for j in (2 * p, 2 * p + 1):
                k = j % 2
                *key, bank = s_bank(b, slot, p, k)
                if ("smax", *key) in T:
                    need(pe, T["smax", *key])
                q0 = 512 * g + 128 * t
                T["s_pe", k] = cp.mark(pe.matmul(bank[:], tile[32 * j:32 * j + 24, 0, q0:q0 + 128],
                                                 tile[32 * j:32 * j + 24, 1, 512 * g:512 * g + 512],
                                                 start=True, stop=True))

        def row_max(b, slot, p, k):
            g, t = divmod(slot, 4)
            need(dve, T["s_pe", k])
            if b >= 2 and slot == 0:
                need(dve, T["mx_pe", b - 2])
            c = 4 * (2 * p + k) + g
            *key, bank = s_bank(b, slot, p, k)
            T["smax", *key] = cv.mark(dve.tensor_reduce(mx[b % 2][:, t, c:c + 1], bank[:], X, ALU.max))
            T["max", b] = T["smax", *key]

        def maxima(b):
            i = b % 2
            yield from m_take()
            need(pe, T["max", b])
            need(pe, T["w", 1])
            for t in range(4):
                mm = pe.transpose(psM[0:16, 128 * t:128 * t + 128], mx[i][:, t, :], ident[:])
            T["mx_pe", b] = cp.mark(mm)
            yield 1
            need(dve, T["mx_pe", b])
            if b > 0:
                need(dve, T["mw", b - 1])
            a = cv.mark(dve.tensor_scalar(mh[:, 0, :], psM[0:16, :], -1.0, None, ALU.mult))
            yield 1
            need(dve, a)
            T["mh", b] = cv.mark(dve.scalar_tensor_tensor(out=mh[:, 1, :], in0=psM[0:16, :], scalar=-1.0,
                                                          in1=mh[:, 0, :], op0=ALU.mult, op1=ALU.subtract))
            T["M"] = T["mh", b]
            need(sp, T["mh", b])
            if b >= 2:
                need(sp, T["mr", b - 2])
            T["mw", b] = d_mw[i].mark(sp.dma_start(m_dram[i], mh[:].bitcast(F32)))
            need(sp, T["mw", b])
            md = m_dram[i].rearrange("(j g) n q -> n j g q", g=4)
            for n in range(2):
                T["mr", b] = d_mr[i].mark(sp.dma_start(
                    QK[i][24 + n:128:32, 0, :].rearrange("p (g q) -> p g q", g=4).bitcast(F32), md[n]))

        def st_pair(b, slot, p):
            g, kt = divmod(slot, 4)
            tile = QK[b % 2]
            need(pe, T["mr", b])
            for j in (2 * p, 2 * p + 1):
                k = j % 2
                if b == 0 and slot == 0:
                    need(pe, T["max", 0])
                if ("exp", k) in T:
                    need(pe, T["exp", k])
                k0 = 512 * g + 128 * kt
                T["t_pe", k] = cp.mark(pe.matmul(psT[k][:], tile[32 * j:32 * j + 26, 1, k0:k0 + 128],
                                                 tile[32 * j:32 * j + 26, 0, 512 * g:512 * g + 512],
                                                 start=True, stop=True))
            T["st_pe", b, slot] = T["t_pe", 1]

        def exp_pair(b, slot, p):
            for j in (2 * p, 2 * p + 1):
                k = j % 2
                need(act, T["t_pe", k])
                ring = (slot * 4 + j) % 8
                need(act, T["pring", ring] if ("pring", ring) in T else T["split", 4])
                T["exp", k] = ca.mark(act.activation(P[:, ring, :], psT[k][:], ACT.Exp))
                T["p", b, slot, j] = (T["exp", k], ring)

        def weighted(b, slot):
            g, kt = divmod(slot, 4)
            need(pe, T["v", b])
            if kt == 0 and "oe" in T:
                need(pe, T["oe"])
            for j in range(4):
                tok, ring = T["p", b, slot, j]
                need(pe, tok)
                mm = pe.matmul(psO[32 * j:32 * j + 16, :], V[b % 2][:, kt, 4 * g + j, :], P[:, ring, :],
                               start=kt == 0, stop=kt == 3)
            tok = cp.mark(mm)
            for j in range(4):
                T["pring", T["p", b, slot, j][1]] = tok
            if kt == 3:
                T["pv_pe", b, g] = tok
                need(act, tok)
                if ("og", g % 2) in T:
                    need(act, T["og", g % 2])
                T["oe"] = ca.mark(act.copy(Oe[:, g % 2, :], psO[:]))
                need(sp, T["oe"])
                if b > 0 and g == 0:
                    need(sp, T["norm", b - 1])
                for j in range(4):
                    r = 32 * g + 8 * j
                    d_o[g % 2].mark(sp.dma_start(Oc[r:r + 8, :], Oe[32 * j:32 * j + 8, g % 2, :]))
                    T["og", g % 2] = d_o[g % 2].mark(sp.dma_start(Dc[r:r + 8, :], Oe[32 * j + 8:32 * j + 16, g % 2, :]))

        def rstd(n, mv):
            ve, rs, nt = sml[n][:, 0, :], sml[n][:, 1, :], sml[n][:, 2, :]

            def do(ins):
                a = cv.mark(ins)
                return a

            a = do(dve.tensor_scalar(ve, mv[:, :, 1], EPS, None, ALU.add))
            yield 1
            need(dve, a)
            a = do(dve.tensor_scalar(rs.bitcast(I32), ve.bitcast(I32), 1, None, ALU.logical_shift_right))
            yield 1
            need(dve, a)
            a = do(dve.tensor_scalar(rs.bitcast(I32), rs.bitcast(I32), -1, MAGIC, ALU.mult, ALU.add))
            for _ in range(3):
                yield 1
                need(dve, a)
                a = do(dve.tensor_tensor(nt, rs, rs, ALU.mult))
                yield 1
                need(dve, a)
                a = do(dve.scalar_tensor_tensor(out=nt, in0=nt, scalar=-0.5, in1=ve, op0=ALU.mult, op1=ALU.mult))
                yield 1
                need(dve, a)
                a = do(dve.scalar_tensor_tensor(out=rs, in0=nt, scalar=1.5, in1=rs, op0=ALU.add, op1=ALU.mult))
            T["rs", n] = a

        def layer_norm(n, engine, counter, dst, src, ready, free):
            st, mv = stat[n], mvs[n]
            need(dve, ready)
            if ("ln", n) in T:
                need(dve, T["ln", n])
            for t in range(4):
                a = cv.mark(dve.bn_stats(st[:, t, :], src[:, t, :]))
            yield 1
            need(dve, a)
            for t in range(4):
                a = cv.mark(dve.bn_aggr(mv[:, t, :], st[:, t, :]))
            yield 1
            need(dve, a)
            yield from rstd(n, mv)
            yield 1
            need(engine, T["rs", n])
            for tok in free:
                need(engine, tok)
            for t in range(4):
                a = counter.mark(engine.tensor_scalar(dst[:, t, :], src[:, t, :], mv[:, t, 0:1],
                                                      sml[n][:, 1, t:t + 1], ALU.subtract, ALU.mult))
            T["ln", n] = a

        def over(ap):
            return ap.unsqueeze(2).to_broadcast([128, 4, 8])

        def chain(b):
            i = b % 2
            need(dve, T["og", 0])
            need(dve, T["og", 1])
            if b > 0:
                need(dve, T["log_pe", b - 1])
            for t in range(4):
                c = slice(128 * t, 128 * t + 128)
                a = cv.mark(dve.reciprocal(Dc[:, c], Dc[:, c]))
                yield 1
                need(dve, a)
                T["norm", b] = cv.mark(dve.tensor_tensor(On[:, c], Oc[:, c], Dc[:, c], ALU.mult))
            yield Y_OUT
            yield from m_take()
            need(pe, T["norm", b])
            need(pe, T["w", 2])
            for t in range(4):
                mm = pe.matmul(psM[:, 128 * t:128 * t + 128], On[:, 128 * t:128 * t + 128], wos[:],
                               start=True, stop=True)
            T["out_pe", b] = cp.mark(mm)
            yield 2
            need(dve, T["out_pe", b])
            need(dve, T["xb", b])
            if ("ln", 1) in T:
                need(dve, T["ln", 1])
            T["r1", b] = cv.mark(dve.tensor_tensor(R[:], psM[:].rearrange("p (t d) -> p t d", t=4), xr[:], ALU.add))
            T["M"] = T["r1", b]
            yield 1
            yield from layer_norm(0, dve, cv, x1[i], R, T["r1", b], [T["x1_last", b - 2]] if b >= 2 else [])
            T["x1", b] = T["ln", 0]
            yield Y_X1
            yield from m_take()
            need(pe, T["x1", b])
            for t in range(4):
                mm = pe.transpose(psM[:, 128 * t:128 * t + 128], x1[i][:, t, :], ident[:])
            T["x1_pe", b] = cp.mark(mm)
            yield 1
            need(dve, T["x1_pe", b])
            if b >= 2:
                need(dve, T["h_pe", b - 2])
            a = cv.mark(dve.tensor_copy(x1h[i][:], psM[:]))
            yield 1
            need(dve, a)
            T["x1l", b] = cv.mark(dve.tensor_tensor(x1l[i][:], psM[:], x1h[i][:], ALU.subtract))
            yield 1
            T["x1T", b] = cv.mark(dve.tensor_copy(x1T[:], psM[:]))
            T["M"] = T["x1T", b]
            yield Y_ROUTE

            yield from m_take()
            need(pe, T["x1T", b])
            need(pe, T["w", 5])
            for t in range(4):
                mm = pe.matmul(psM[:, 8 * t:8 * t + 8], x1T[:, 128 * t:128 * t + 128], wrs[:], start=True, stop=True)
            T["log_pe", b] = cp.mark(mm)
            yield 1
            need(dve, T["log_pe", b])
            need(dve, T["w", 5])
            dsc = desc[:].rearrange("p (t e) -> p t e", t=4)
            a = cv.mark(dve.tensor_tensor(lg[:], psM[:, 0:32].rearrange("p (t e) -> p t e", t=4),
                                          brs[:].unsqueeze(1).to_broadcast([128, 4, 8]), ALU.add))
            T["M"] = a
            for n, (l, oh) in enumerate(((lg, oh1), (l2, oh2))):
                yield 1
                need(dve, a)
                a = cv.mark(dve.tensor_reduce(rm[:, 2 * n, :], l[:], X, ALU.max))
                need(dve, a)
                a = cv.mark(dve.tensor_tensor(e1[:], l[:], over(rm[:, 2 * n, :]), ALU.is_ge))
                yield 1
                need(dve, a)
                a = cv.mark(dve.tensor_tensor(t1[:], e1[:], dsc, ALU.mult))
                need(dve, a)
                a = cv.mark(dve.tensor_reduce(rm[:, 2 * n + 1, :], t1[:], X, ALU.max))
                yield 1
                need(dve, a)
                a = cv.mark(dve.tensor_tensor(oh[:], t1[:], over(rm[:, 2 * n + 1, :]), ALU.is_equal))
                if n == 0:
                    need(dve, a)
                    a = cv.mark(dve.scalar_tensor_tensor(out=l2[:], in0=oh1[:], scalar=-3e38, in1=lg[:],
                                                         op0=ALU.mult, op1=ALU.add))
            T["gap"] = cv.mark(dve.tensor_tensor(rm[:, 4, :], rm[:, 2, :], rm[:, 0, :], ALU.subtract))
            yield 1
            need(act, T["gap"])
            T["gexp"] = ca.mark(act.activation(rm[:, 5, :], rm[:, 4, :], ACT.Exp))
            yield 3
            need(dve, T["gexp"])
            a = cv.mark(dve.tensor_scalar(rm[:, 6, :], rm[:, 5, :], 1.0, None, ALU.add))
            need(dve, a)
            a = cv.mark(dve.reciprocal(rm[:, 6, :], rm[:, 6, :]))
            yield 1
            need(dve, a)
            a = cv.mark(dve.tensor_tensor(rm[:, 7, :], rm[:, 5, :], rm[:, 6, :], ALU.mult))
            cv.mark(dve.tensor_tensor(oh1[:], oh1[:], over(rm[:, 6, :]), ALU.mult))
            yield 1
            need(dve, a)
            a = cv.mark(dve.tensor_tensor(oh2[:], oh2[:], over(rm[:, 7, :]), ALU.mult))
            yield 1
            need(dve, a)
            if b > 0:
                need(dve, T["wT_pe", b - 1])
            T["wt", b] = cv.mark(dve.tensor_tensor(wt[:], oh1[:], oh2[:], ALU.add))
            yield Y_WT
            yield from m_take()
            need(pe, T["wt", b])
            for t in range(4):
                mm = pe.transpose(psM[0:8, 128 * t:128 * t + 128], wt[:, t, :], ident[:])
            T["wT_pe", b] = cp.mark(mm)
            yield 1
            need(act, T["wT_pe", b])
            if b > 0:
                need(act, T["ww", b - 1])
            T["wT", b] = ca.mark(act.copy(wTs[:], psM[0:8, :]))
            T["M"] = T["wT", b]
            need(sp, T["wT", b])
            if b >= 2:
                for k in range(3):
                    need(sp, T["wb", b - 2, 5 + k])
            T["ww", b] = d_ww[i].mark(sp.dma_start(w_dram[i], wTs[:]))

        def weight_rows(b, e):
            k = (8 * b + e) % 3
            need(sp, T["ww", b])
            if ("wfree", k) in T:
                need(sp, T["wfree", k])
            T["wb", b, e] = d_wb[k].mark(sp.dma_start(Wb[k][:], rows(w_dram[b % 2][e])))

        def hidden(b, m, alone, late):
            i = b % 2
            n = 32 * b + m
            if alone:
                T.setdefault("alone", n)
            need(pe, T["x1l", b])
            need(pe, T["split", 4])
            bank = (psH, psS[0], psS[1])[n % 3 if alone else 0]
            before = ("relu", n - 3 if alone and n >= T["alone"] + 3 else n - 1)
            if alone and n == T["alone"]:
                need(pe, T["max", NB - 1])
            if before in T:
                need(pe, T[before])
            c = slice(128 * m, 128 * m + 128)
            pe.matmul(bank[:], w1h[:, c], x1l[i][:], start=True, stop=False)
            pe.matmul(bank[:], w1l[:, c], x1h[i][:], start=False, stop=False)
            T["h_pe", b] = cp.mark(pe.matmul(bank[:], w1h[:, c], x1h[i][:], start=False, stop=True))
            need(act, T["h_pe", b])
            need(act, T["w", 5])
            if ("low", n - 3) in T:
                need(act, T["low", n - 3])
            if ("y_pe", n - 5) in T:
                need(act, T["y_pe", n - 5])
            if n == 0:
                need(act, T["qw", 0])
            ca.mark(act.activation(hF[:, n % 3, :], bank[:], ACT.Relu, bias=b1s[:, m:m + 1]))
            T["relu", n] = ca.mark(act.activation(hH[:, n % 5, :], bank[:], ACT.Relu, bias=b1s[:, m:m + 1]))
            T["low next"] = (n, late)

        def low():
            if "low next" not in T:
                return
            n, late = T.pop("low next")
            engine, counter = (dve, cv) if late and n % 4 else (pool, cg)
            need(engine, T["relu", n])
            if n == 0:
                need(engine, T["qw", 0])
            if ("y_pe", n - 5) in T:
                need(engine, T["y_pe", n - 5])
            T["low", n] = counter.mark(engine.tensor_tensor(hL[:, n % 5, :], hF[:, n % 3, :], hH[:, n % 5, :],
                                                            ALU.subtract))

        def experts(b, m):
            n = 32 * b + m
            e, f = divmod(m, 4)
            need(pe, T["low", n])
            if f == 0 and "yw" in T:
                need(pe, T["yw"])
            c = slice(128 * m, 128 * m + 128)
            pe.matmul(psY[:], w2h[:, c], hL[:, n % 5, :], start=f == 0, stop=False)
            pe.matmul(psY[:], w2l[:, c], hH[:, n % 5, :], start=False, stop=False)
            T["y_pe", n] = cp.mark(pe.matmul(psY[:], w2h[:, c], hH[:, n % 5, :], start=False, stop=f == 3))
            if f == 3:
                T["y_last"] = T["y_pe", n]

        def weigh(b, e):
            i = b % 2
            k = (8 * b + e) % 3
            need(dve, T["y_last"])
            need(dve, T["wb", b, e])
            if e == 0:
                if b >= 2:
                    need(dve, T["fin_pe", b - 2])
                dst = accT[i]
            else:
                dst = tt
                if "ttfree" in T:
                    need(dve, T["ttfree"])
            T["yw"] = cv.mark(dve.scalar_tensor_tensor(out=dst[:], in0=psY[:], scalar=b2s[:, e:e + 1], in1=Wb[k][:],
                                                       op0=ALU.add, op1=ALU.mult))
            T["wfree", k] = T["yw"]
            if e > 0:
                need(pool, T["yw"])
                if e > 1:
                    need(pool, T["ttfree"])
                T["ttfree"] = cg.mark(pool.tensor_tensor(accT[i][:], accT[i][:], dst[:], ALU.add))
                T["acc", b] = T["ttfree"]
            T["weighed"] = 8 * b + e + 1

        def finish(b):
            i = b % 2
            yield from m_take()
            need(pe, T["acc", b])
            for t in range(4):
                mm = pe.transpose(psM[:, 128 * t:128 * t + 128], accT[i][:, 128 * t:128 * t + 128], ident[:])
            T["fin_pe", b] = cp.mark(mm)
            yield 2
            need(dve, T["fin_pe", b])
            need(dve, T["ln", 0])
            a = cv.mark(dve.tensor_tensor(F[:], psM[:].rearrange("p (t d) -> p t d", t=4), x1[i][:], ALU.add))
            T["M"] = a
            engine, counter = (dve, cv) if b >= NB - 2 else (pool, cg)
            need(pool, T["x1_pe", b])
            need(pool, a)
            T["x1b"] = cg.mark(pool.tensor_tensor(x1[i][:], x1[i][:], be[:].unsqueeze(1).to_broadcast([128, 4, 128]),
                                                  ALU.add))
            yield 1
            yield from layer_norm(1, engine, counter, fin, F, a, [T["out", b - 1]] if b > 0 else [])
            a = T["ln", 1]
            need(engine, a)
            need(engine, T["w", 5])
            a = counter.mark(engine.tensor_tensor(fin[:], fin[:], ga[:].unsqueeze(1).to_broadcast([128, 4, 128]),
                                                  ALU.mult))
            need(engine, a)
            need(engine, T["x1b"])
            a = counter.mark(engine.tensor_tensor(fin[:], fin[:], x1[i][:], ALU.add))
            T["x1_last", b] = a
            yield 20 if b < NB - 1 else 1
            yield from layer_norm(2, engine, counter, fin, fin, a, [])
            need(sp, T["ln", 2])
            T["out", b] = d_out[i].mark(sp.dma_start(out_v[b], fin[:]))

        running = []

        def begin(task):
            running.append([task, 0])

        def tick():
            for item in list(running):
                if item[1] > 0:
                    item[1] -= 1
                    continue
                pause = next(item[0], None)
                if pause is None:
                    running.remove(item)
                else:
                    item[1] = pause - 1

        ahead = 0
        need(pe, T["w", 1])
        need(act, T["v1", 1])
        need(pe, T["x", 0])
        split(3, w1h, w1l)
        steps = []
        for G in range(-16, HS * NB + T_H + LAG + 28):
            steps.append((G, G - T_H if G >= T_H else None))
        for G, M in steps:
            if M is not None and M >= M_FIN and (M - M_FIN) % HS == 0 and (M - M_FIN) // HS < NB:
                begin(finish((M - M_FIN) // HS))
            for b in range(NB):
                s = G - HS * b
                if s == T_XIN:
                    x_in(b)
                if s == T_HALF:
                    spread(b, 1)
                if s == T_XR:
                    residual_in(b)
                for at, task in ((T_Q, lambda: project(b, 0)), (T_K, lambda: project(b, 1)), (T_V, lambda: values(b)),
                                 (T_MX, lambda: maxima(b)), (T_CHAIN, lambda: chain(b))):
                    if s == at:
                        begin(task())
            if G in DUMMY:
                need(pe, T["w1h"])
                for _ in range(DUMMY[G]):
                    pe.matmul(psY[:], w1h[:, 0:128], w1h[:, 0:512], start=True, stop=True)
            if G == 0:
                split_second()
            of = {}
            for name, clock, at in (("s", G, 0), ("st", G, T_ST), ("pv", G, T_ST + 2), ("h", M, 0), ("y", M, LAG)):
                if clock is not None and 0 <= clock - at < HS * NB:
                    of[name] = divmod(clock - at, HS)
            if M is not None and M - LAG > 0 and (M - LAG) % 4 == 0 and (M - LAG) // 4 <= 8 * NB:
                of["w"] = divmod((M - LAG) // 4 - 1, 8)
            if "w" in of:
                weigh(*of["w"])
            if ahead < 8 * NB and ("ww", ahead // 8) in T and T.get("weighed", 0) >= ahead - 2:
                weight_rows(*divmod(ahead, 8))
                ahead += 1
            if "st" in of:
                b, m = of["st"]
                st_pair(b, m // 2, m % 2)
                exp_pair(b, m // 2, m % 2)
            if "pv" in of and of["pv"][1] % 2 == 0:
                weighted(of["pv"][0], of["pv"][1] // 2)
            low()
            tick()
            if "h" in of:
                hidden(*of["h"], G > HS * NB, "st" not in of)
            if "s" in of:
                b, m = of["s"]
                s_pair(b, m // 2, m % 2)
                for k in range(2):
                    row_max(b, m // 2, m % 2, k)
                    tick()
            else:
                tick()
                tick()
            if "y" in of:
                experts(*of["y"])
            tick()
        assert not running
        for b in range(NB - 2, NB):
            need(sp, T["out", b])
            need(sp, T["qw", b])
            need(sp, T["mw", b])
            need(sp, T["ww", b])


def _constants():
    n = np.arange(8)
    k = (n[:, None] - n[None, :]) % 8
    basis = np.zeros((128, 5, 128), np.float32)
    for f in range(5):
        c = np.cos(2 * np.pi * f * k / 8) / 8 * (1 if f in (0, 4) else 2)
        for g in range(4):
            for j in range(4):
                h = 4 * g + j
                for a in range(8):
                    for d in range(8):
                        basis[8 * h + a, f, 32 * j + 4 * d + g] = c[a, d]
    desc = np.tile(np.arange(8, 0, -1, dtype=np.float32), (128, 4))
    return basis.reshape(128, 640), np.eye(128, dtype=np.float32), np.ascontiguousarray(desc)


def kernel(**inputs):
    import concourse.bacc as bacc
    from concourse.bass_utils import run_bass_kernel_spmd

    a = {k: np.asarray(v) for k, v in inputs.items()}
    x = a["L0_attn_x"]
    wqkv = a["L0_attn_w_qkv"]
    W1, W2, b1 = a["L0_ffn_W1"], a["L0_ffn_W2"], a["L0_ffn_b1"]
    basis, ident, desc = _constants()
    arrays = {
        "x": x,
        "xT": x.reshape(4096, 128).T,
        "wqkvT": np.concatenate([wqkv[:, 0:128].T, wqkv[:, 128:256].T], axis=1),
        "wv": wqkv[:, 256:384],
        "w_out": a["L0_attn_w_out"],
        "b_out": a["L0_attn_b_out"],
        "mlog": a["L0_attn_mask_logits"],
        "wrT": a["L0_ffn_Wr"].T,
        "br": a["L0_ffn_br"],
        "w1T": W1.reshape(4096, 128).T,
        "b1T": b1.reshape(32, 128).T,
        "w2T": W2.transpose(0, 2, 1).reshape(32, 128, 128).transpose(1, 0, 2).reshape(128, 4096),
        "b2T": a["L0_ffn_b2"].T,
        "gamma": a["L0_ffn_gamma"],
        "beta": a["L0_ffn_beta"],
        "basis": basis, "ident_c": ident, "desc_c": desc,
    }
    arrays = {f"in_{k}": np.ascontiguousarray(v) for k, v in arrays.items()}
    nc = bacc.Bacc("TRN2", target_bir_lowering=False, num_devices=1)
    args = [nc.dram_tensor(n, v.shape, mybir.dt.from_np(v.dtype), kind="ExternalInput").ap() for n, v in arrays.items()]
    args.append(nc.dram_tensor("out_dram", (8, 512, 128), F32, kind="ExternalOutput").ap())
    build_program(nc, *args)
    r = run_bass_kernel_spmd(nc, [arrays], core_ids=[0])
    return r.results[0]["out_dram"]
```
